# Optimizing a Trainium2 kernel written in Bass

```python
import numpy as np
import jax
import jax.numpy as jnp

def _softmax(x, axis=-1):
    return jax.nn.softmax(x, axis=axis)

def _gelu(x):
    return jax.nn.gelu(x, approximate=True)

def _silu(x):
    return jax.nn.silu(x)

def _sigmoid(x):
    return jax.nn.sigmoid(x)

def _layernorm(x, axis=-1, eps=1e-05):
    m = jnp.mean(x, axis=axis, keepdims=True)
    v = jnp.var(x, axis=axis, keepdims=True)
    return (x - m) / jnp.sqrt(v + eps)

def _scatter_add(tgt, idx, src, axis=0):
    return tgt.at[idx].add(src)

def _segment_sum(src, seg, n):
    return jax.ops.segment_sum(src, seg, n)
kernel_name = 'mk_gnn_preln_d1_gnn_r32_100a69'

def setup_inputs(seed: int=0):
    np.random.seed(seed)
    _w = jnp.asarray

    def _rec_inputs():
        import jax
        import jax.numpy as jnp
        _gk = jax.random.key(seed)
        x = -0.0001006 + 1 * jax.random.normal(jax.random.fold_in(_gk, 1), (50000, 96), jnp.float32)
        src = jax.random.randint(jax.random.fold_in(_gk, 2), (25000,), 0, 50000, jnp.int32)
        dst = jax.random.randint(jax.random.fold_in(_gk, 3), (25000,), 0, 50000, jnp.int32)
        _o = jnp.argsort(dst, stable=True)
        src = src[_o]
        dst = dst[_o]
        edge_attr_96 = 5.93493e-05 + 1.00006 * jax.random.normal(jax.random.fold_in(_gk, 11), (25000, 96), jnp.float32)
        return (x, src, dst, edge_attr_96)
    x, src, dst, edge_attr_96 = _rec_inputs()

    def _L0_gnn_setup():
        import jax, jax.numpy as jnp
        import numpy as np
        N_NODES = 50000
        N_EDGES = 25000
        IN_DIM = 96
        NUM_HEADS = 8
        HEAD_DIM = IN_DIM // NUM_HEADS
        key = jax.random.key(seed)
        ks = jax.random.split(key, 11)
        s = 1.0 / np.sqrt(IN_DIM)
        return {'x': jax.random.normal(ks[0], (N_NODES, IN_DIM), dtype=jnp.float32), 'edge_index': jax.random.randint(ks[1], (2, N_EDGES), 0, N_NODES, dtype=jnp.int64), 'edge_attr': jax.random.normal(ks[2], (N_EDGES, IN_DIM), dtype=jnp.float32), 'Wq': jax.random.normal(ks[3], (IN_DIM, IN_DIM), dtype=jnp.float32) * s, 'bq': jax.random.normal(ks[4], (IN_DIM,), dtype=jnp.float32) * s, 'Wk': jax.random.normal(ks[5], (IN_DIM, IN_DIM), dtype=jnp.float32) * s, 'bk': jax.random.normal(ks[6], (IN_DIM,), dtype=jnp.float32) * s, 'We': jax.random.normal(ks[7], (IN_DIM, IN_DIM), dtype=jnp.float32) * s, 'be': jax.random.normal(ks[8], (IN_DIM,), dtype=jnp.float32) * s, 'Wv': jax.random.normal(ks[9], (IN_DIM, IN_DIM), dtype=jnp.float32) * s, 'bv': jax.random.normal(ks[10], (IN_DIM,), dtype=jnp.float32) * s}
    _L0_gnn_all = _L0_gnn_setup()
    _L0_gnn_in = {k: v for k, v in _L0_gnn_all.items() if k in ('Wq', 'bq', 'Wk', 'bk', 'We', 'be', 'Wv', 'bv')}
    del _L0_gnn_all
    return {'x': x, 'src': src, 'dst': dst, 'edge_attr_96': edge_attr_96, 'L0_gnn_Wq': _L0_gnn_in['Wq'], 'L0_gnn_bq': _L0_gnn_in['bq'], 'L0_gnn_Wk': _L0_gnn_in['Wk'], 'L0_gnn_bk': _L0_gnn_in['bk'], 'L0_gnn_We': _L0_gnn_in['We'], 'L0_gnn_be': _L0_gnn_in['be'], 'L0_gnn_Wv': _L0_gnn_in['Wv'], 'L0_gnn_bv': _L0_gnn_in['bv']}

def reference(x, src, dst, edge_attr_96, L0_gnn_Wq, L0_gnn_bq, L0_gnn_Wk, L0_gnn_bk, L0_gnn_We, L0_gnn_be, L0_gnn_Wv, L0_gnn_bv):
    import jax
    import jax.numpy as jnp

    def _L0_gnn_ref(x, edge_index, edge_attr, Wq, bq, Wk, bk, We, be, Wv, bv):
        import jax, jax.numpy as jnp
        import numpy as np
        N_NODES = 50000
        N_EDGES = 25000
        IN_DIM = 96
        NUM_HEADS = 8
        HEAD_DIM = IN_DIM // NUM_HEADS
        N = x.shape[0]
        H, D = (NUM_HEADS, HEAD_DIM)
        Q_h = (x @ Wq + bq).reshape(N, H, D)
        K_h = (x @ Wk + bk).reshape(N, H, D)
        V_h = (x @ Wv + bv).reshape(N, H, D)
        E = (edge_attr @ We + be).reshape(-1, H, D)
        src_idx = edge_index[0]
        dst_idx = edge_index[1]
        src = K_h[src_idx]
        dest = Q_h[dst_idx]
        score = src * dest / jnp.sqrt(jnp.asarray(D, x.dtype))
        score = score * E
        score = jnp.exp(jnp.clip(score.sum(-1, keepdims=True), -5.0, 5.0))
        msg = V_h[src_idx] * score
        wV = jax.ops.segment_sum(msg, dst_idx, num_segments=N)
        Z = jax.ops.segment_sum(score, dst_idx, num_segments=N)
        h_out = wV / (Z + 1e-06)
        return h_out.reshape(N, H * D)
    edge_index = jnp.stack([src, dst])
    h = jnp.maximum(_layernorm(x, axis=-1), 0.0)
    x = x + _L0_gnn_ref(h, edge_index, edge_attr_96, L0_gnn_Wq, L0_gnn_bq, L0_gnn_Wk, L0_gnn_bk, L0_gnn_We, L0_gnn_be, L0_gnn_Wv, L0_gnn_bv)
    return x

_drawn_inputs = setup_inputs


def setup_inputs(seed=0):
    import zlib

    import numpy as np

    out = dict(_drawn_inputs(seed))
    spreads = {}
    factors = {'L0_gnn_bq': 8.0, 'L0_gnn_bk': 8.0, 'L0_gnn_be': 8.0}
    for name, (base, spread) in spreads.items():
        noise = np.random.default_rng([zlib.crc32(name.encode()), seed]).standard_normal(out[name].shape)
        drawn = base * np.exp(spread * noise) if base else spread * noise
        out[name] = jnp.asarray(drawn.astype(out[name].dtype))
    for name, factor in factors.items():
        out[name] = (out[name] * factor).astype(out[name].dtype)
    return out
```

```python
import concourse.bass as bass
from concourse import mybir
from contextlib import ExitStack


def gnn_edge_attention(nc, x, src, dst, edge_attr, wq, bq, wk, bk, we, be, wv, bv, out):
    f32 = mybir.dt.float32
    i32 = mybir.dt.int32
    ALU = mybir.AluOpType
    ACT = mybir.ActivationFunctionType
    AX = mybir.AxisListType.X

    P = 128
    N, D = x.shape
    E = src.shape[0]
    H = 8
    HD = D // H
    C = D + H
    COLS = E // P
    REST = E - P * COLS
    TILES = COLS + 1
    PAIRS = 14
    LAP = 2 * PAIRS
    HALF = LAP // 2
    LAPS = TILES // LAP
    SKIP = 1 << 20
    EPS = 1e-5
    assert TILES == LAPS * LAP and REST > 0 and D == H * HD
    W4 = 4 * D
    CHUNKS = 4
    FN = 125
    FG = 14
    FTILES = N // FN
    assert N % FN == 0 and TILES % (2 * FG) == 0

    ctx = ExitStack()
    with ctx:
        def sb(name, shape, dt=f32):
            return ctx.enter_context(nc.sbuf_tensor(name, shape, dt))

        def sem(name):
            return ctx.enter_context(nc.semaphore(name))

        idx = sb("idx", [P, 2, TILES], i32)
        nxt = sb("nxt", [P, TILES], i32)
        put = sb("put", [P, TILES], i32)
        dstf = sb("dstf", [P, TILES])
        nxtf = sb("nxtf", [P, TILES])
        mask = sb("mask", [P, TILES])
        goes_on = sb("goes_on", [P, TILES])
        in_head = sb("in_head", [P, TILES])
        take = [sb(f"take{h}", [P, 2, HALF], i32) for h in range(2)]
        give = [sb(f"give{h}", [P, HALF], i32) for h in range(2)]
        xs = sb("xs", [P, LAP, D])
        xd = sb("xd", [P, LAP, D])
        ea = sb("ea", [P, LAP, D])
        rows = sb("rows", [P, LAP, D])
        stats = sb("stats", [P, 2, 4, 6])
        mv = sb("mv", [P, 2, 4, 2])
        lnv = sb("lnv", [P, 2, 4])
        rst0 = sb("rst0", [P, 2, 4])
        nwt = sb("nwt", [P, 2, 2, 4])
        rstd = sb("rstd", [P, 2, 4])
        nmr = sb("nmr", [P, 2, 4])
        hb = sb("hb", [P, 2, 4, D])
        tT = sb("tT", [D + 1, 2, 2, 3 * P])
        qs = sb("qs", [P, 2, 2, D])
        kq = sb("kq", [P, 2, 2, D])
        kqe = sb("kqe", [P, 2, 2, D])
        ssum = sb("ssum", [P, 2, 2, H])
        clip = sb("clip", [P, 2, 2, H])
        msg = sb("msg", [P, 2, 2, C])
        zeps = sb("zeps", [P, 2, 2, H])
        zinv = sb("zinv", [P, 2, 2, H])
        hout = sb("hout", [P, 2, 2, D])
        run = sb("run", [P, (TILES + 1) * C])
        head = sb("head", [P, 2, C])
        w_all = sb("w_all", [D + 1, W4])
        ident = sb("ident", [P, P])
        ones = sb("ones", [P, P])
        before = sb("before", [P, P])
        eps = sb("eps", [P, 1])
        pi = sb("pi", [P, 1], i32)
        pf = sb("pf", [P, 1])
        neg = sb("neg", [P, 3])
        real = sb("real", [P, 2])
        dif = sb("dif", [P, 2])
        viol = sb("viol", [P, 1])
        bad = sb("bad", [P, 1], i32)
        sorted_ = sb("sorted_", [P, 1])
        ids = sb("ids", [P, 3])
        diag = sb("diag", [P, 3, P])
        eq = sb("eq", [P, 3, 3 * P])
        eqb = sb("eqb", [P, 3, P])
        rmat = sb("rmat", [P, 3, C])
        rx = sb("rx", [P, 3, D])
        rz = sb("rz", [P, 2, 3, H])
        rh = sb("rh", [P, 3, D])
        rrow = sb("rrow", [P, 3, D])
        rsel = sb("rsel", [P, 4, 3])
        rput = sb("rput", [P, 3], i32)
        nodei = sb("nodei", [P, FN], i32)
        node = sb("node", [P, FN])
        left = sb("left", [P, TILES])
        hot = [sb(f"hot{b}", [P, FG, FN]) for b in range(2)]
        fx = sb("fx", [FN, D])
        fz = sb("fz", [FN, 2, H])
        fh = sb("fh", [FN, D])
        fo = sb("fo", [FN, D])

        ps_t = ctx.enter_context(nc.psum_tensor("ps_t", [P, 2, 2, 512], f32))
        ps_p = ctx.enter_context(nc.psum_tensor("ps_p", [P, 2, 2, 512], f32))

        blank = sem("blank")
        idx_in = sem("idx_in")
        w_in = sem("w_in")
        copied = sem("copied")
        ea_in = [sem(f"ea_in{h}") for h in range(2)]
        rest_in = sem("rest_in")
        gathered = [sem(f"gathered{j}") for j in range(PAIRS)]
        scattered = [sem(f"scattered{j}") for j in range(PAIRS)]
        taken = sem("taken")
        staged = sem("staged")
        made = sem("made")
        prep = sem("prep")
        pre = sem("pre")
        viol_in = sem("viol_in")
        viol_sum = sem("viol_sum")
        stat_s = sem("stat_s")
        stat_ok = sem("stat_ok")
        passed = sem("passed")
        ln_ok = sem("ln_ok")
        rst0_ok = sem("rst0_ok")
        nw0 = sem("nw0")
        nw1 = sem("nw1")
        nw1b = sem("nw1b")
        rstd_ok = sem("rstd_ok")
        norm_ok = sem("norm_ok")
        h_ok = sem("h_ok")
        turned = sem("turned")
        t_ok = sem("t_ok")
        proj_ok = sem("proj_ok")
        q_ok = sem("q_ok")
        kq_ok = sem("kq_ok")
        kqe_ok = sem("kqe_ok")
        sum_ok = sem("sum_ok")
        clip_ok = sem("clip_ok")
        exp_ok = sem("exp_ok")
        msg_ok = sem("msg_ok")
        run0_ok = sem("run0_ok")
        run1_ok = sem("run1_ok")
        head0_ok = sem("head0_ok")
        head_ok = sem("head_ok")
        zeps_ok = sem("zeps_ok")
        zinv_ok = sem("zinv_ok")
        hout_ok = sem("hout_ok")
        rows_ok = sem("rows_ok")
        rec_in = sem("rec_in")
        rec_x = sem("rec_x")
        rec_ids = sem("rec_ids")
        rec_b = sem("rec_b")
        rec_eq = sem("rec_eq")
        rec_sum = sem("rec_sum")
        rec_step = sem("rec_step")
        rec_ok = sem("rec_ok")
        rec_out = sem("rec_out")
        flag = sem("flag")
        node_ok = sem("node_ok")
        hot_ok = sem("hot_ok")
        hot_free = sem("hot_free")
        facc_ok = sem("facc_ok")
        facc_free = sem("facc_free")
        f_step = sem("f_step")
        fx_in = sem("fx_in")
        fo_ok = sem("fo_ok")
        fo_out = sem("fo_out")

        block = ctx.enter_context(nc.Block())

        def need(eng, s, value):
            if not isinstance(value, int) or value > 0:
                eng.wait_ge(s, value)

        def ahead(o, j, by):
            return (o, j + by) if j + by < PAIRS else (o + 1, j + by - PAIRS)

        @block.sync
        def _(sp):
            sp.wait_ge(blank, 1)
            main = src[0:P * COLS].rearrange("(p t) -> p t", p=P)
            sp.dma_start(idx[:, 0, 0:COLS], main).then_inc(idx_in, 16)
            sp.dma_start(idx[:, 1, 0:COLS], dst[0:P * COLS].rearrange("(p t) -> p t", p=P)).then_inc(idx_in, 16)
            sp.dma_start(idx[0:REST, 0, COLS:TILES], src[P * COLS:E].unsqueeze(1)).then_inc(idx_in, 16)
            sp.dma_start(idx[0:REST, 1, COLS:TILES], dst[P * COLS:E].unsqueeze(1)).then_inc(idx_in, 16)
            sp.dma_start(nxt[:, 0:COLS], dst[1:P * COLS + 1].rearrange("(p t) -> p t", p=P)).then_inc(idx_in, 16)
            sp.dma_start(nxt[0:REST - 1, COLS:TILES], dst[P * COLS + 1:E].unsqueeze(1)).then_inc(idx_in, 16)
            for k, (w, b) in enumerate(((wk, bk), (wv, bv), (wq, bq), (we, be))):
                sp.dma_start(w_all[0:D, k * D:(k + 1) * D], w[:, :]).then_inc(w_in, 16)
                sp.dma_start(w_all[D:D + 1, k * D:(k + 1) * D], b[:].unsqueeze(0)).then_inc(w_in, 16)

            table = edge_attr[0:P * COLS, :].rearrange("(p t) d -> p t d", p=P)

            def load(o, last=False):
                for h in range(2):
                    need(sp, turned, (o - 1) * PAIRS + (h + 1) * PAIRS // 2)
                    n = HALF - 1 if last and h == 1 else HALF
                    sp.dma_start(ea[:, h * HALF:h * HALF + n, :],
                                 table[:, bass.ds(o * LAP + h * HALF, n), :]).then_inc(ea_in[h], 16)
                    if n < HALF:
                        sp.dma_start(ea[0:REST, LAP - 1, :], edge_attr[P * COLS:E, :]).then_inc(rest_in, 16)

            load(0)
            with sp.Fori(1, LAPS - 1) as o:
                load(o)
            load(LAPS - 1, last=True)

            sp.wait_ge(flag, 1)
            unsorted = sp.value_load(bad[0:1, 0:1])
            with sp.If(unsorted != 0):
                sp.wait_ge(copied, 16 * CHUNKS)
                sp.sem_inc(fo_out, 16)
                with sp.Fori(0, FTILES) as n:
                    sp.wait_ge(fo_out, (n + 1) * 16)
                    sp.dma_start(fx[:, :], x[bass.ds(n * FN, FN), :]).then_inc(fx_in, 16)
                    sp.wait_ge(fo_ok, n + 1)
                    sp.dma_start(out[bass.ds(n * FN, FN), :], fo[:, :]).then_inc(fo_out, 16)
                sp.wait_ge(fo_out, (FTILES + 1) * 16)
            sp.wait_ge(copied, 16 * CHUNKS)
            for j in range(PAIRS):
                sp.wait_ge(scattered[j], 32 * LAPS)
            sp.wait_ge(rec_out, 48)

        @block.gpsimd
        def _(pool):
            nc.gpsimd.iota(pi[:, :], [[1, 1]], base=0, channel_multiplier=1)
            nc.gpsimd.iota(nodei[:, :], [[1, FN]], base=0, channel_multiplier=0)
            nc.gpsimd.memset(ones[:, :], 1.0)
            nc.gpsimd.memset(ident[:, :], 0.0)
            nc.gpsimd.memset(before[:, :], 1.0).then_inc(made, 1)
            pool.wait_ge(made, 1)
            nc.gpsimd.affine_select(out=ident[:, :], in_=ident[:, :], compare_op=ALU.not_equal, fill=1.0, base=0,
                                    pattern=[[-1, P]], channel_multiplier=1)
            nc.gpsimd.affine_select(out=before[:, :], in_=before[:, :], compare_op=ALU.is_gt, fill=0.0, base=0,
                                    pattern=[[1, P]], channel_multiplier=-1).then_inc(made, 1)
            pool.wait_ge(idx_in, 96)

            def stage(o, h, gather, scatter):
                if not isinstance(o, int) or o > 0:
                    pool.wait_ge(rows_ok, (o - 1) * PAIRS + (h + 1) * PAIRS // 2)
                    pool.sem_inc(taken, 1)
                if gather:
                    last = nc.gpsimd.tensor_copy(take[h][:, :, :], idx[:, :, bass.ds(o * LAP + h * HALF, HALF)])
                if scatter:
                    last = nc.gpsimd.tensor_copy(give[h][:, :], put[:, bass.ds((o - 1) * LAP + h * HALF, HALF)])
                last.then_inc(staged, 1)
                pool.wait_ge(staged, o * 2 + h + 1)
                pool.sem_inc(taken, 1)

            def lap(o, gather=True, scatter=True):
                for h in range(2):
                    stage(o, h, gather, scatter)
                    for j in range(h * PAIRS // 2, (h + 1) * PAIRS // 2):
                        if scatter:
                            pool.wait_ge(rows_ok, (o - 1) * PAIRS + j + 1)
                            pool.sem_inc(taken, 1)
                        for t in (2 * j, 2 * j + 1):
                            u = t - h * HALF
                            if scatter:
                                nc.gpsimd.indirect_dma_start(
                                    out[:, :], bass.IndirectOffsetOnAxis(ap=give[h][:, u:u + 1], axis=0),
                                    rows[:, t, :], None, bounds_check=N - 1, oob_is_err=False,
                                ).then_inc(scattered[j], 16)
                            if gather:
                                for side, into in ((0, xs), (1, xd)):
                                    nc.gpsimd.indirect_dma_start(
                                        into[:, t, :], None, x[:, :],
                                        bass.IndirectOffsetOnAxis(ap=take[h][:, side, u:u + 1], axis=0),
                                    ).then_inc(gathered[j], 16)

            lap(0, scatter=False)
            pool.wait_ge(copied, 16 * CHUNKS)
            pool.wait_ge(pre, 1)
            pool.sem_inc(taken, 1)
            with pool.Fori(1, LAPS) as o:
                lap(o)
            for g, t in enumerate((0, COLS - 1, COLS)):
                nc.gpsimd.indirect_dma_start(rx[:, g, :], None, x[:, :],
                                             bass.IndirectOffsetOnAxis(ap=idx[:, 1, t:t + 1], axis=0)
                                             ).then_inc(rec_x, 16)
            lap(LAPS, gather=False)
            pool.wait_ge(rec_ok, 1)
            for g in range(3):
                nc.gpsimd.indirect_dma_start(
                    out[:, :], bass.IndirectOffsetOnAxis(ap=rput[:, g:g + 1], axis=0),
                    rrow[:, g, :], None, bounds_check=N - 1, oob_is_err=False).then_inc(rec_out, 16)

        @block.scalar
        def _(act):
            whole = N * D // (CHUNKS * P)
            xc = x.rearrange("n d -> (n d)").rearrange("(c p f) -> c p f", c=CHUNKS, p=P)
            oc = out.rearrange("n d -> (n d)").rearrange("(c p f) -> c p f", c=CHUNKS, p=P)
            for c in range(CHUNKS):
                act.dma_start(oc[c, :, 0:whole], xc[c, :, 0:whole], max_dma_last_dim=4096).then_inc(copied, 16)

            def spread(o, j):
                b = j % 2
                act.wait_ge(stat_ok, o * PAIRS + j + 1)
                nc.scalar.activation(lnv[:, b, :], mv[:, b, :, 1], ACT.Ln, bias=eps[:, :]).then_inc(ln_ok, 1)
                act.wait_ge(ln_ok, o * PAIRS + j + 1)
                nc.scalar.activation(rst0[:, b, :], lnv[:, b, :], ACT.Exp, scale=-0.5).then_inc(rst0_ok, 1)

            def relu(o, j):
                b = j % 2
                act.wait_ge(norm_ok, o * PAIRS + j + 1)
                need(act, turned, o * PAIRS + j - 1)
                for k in range(4):
                    part = (xs, xd)[k // 2][:, 2 * j + k % 2, :]
                    last = nc.scalar.activation(hb[:, b, k, :], part, ACT.Relu, bias=nmr[:, b, k:k + 1],
                                                scale=rstd[:, b, k:k + 1])
                last.then_inc(h_ok, 1)

            def turn(o, j):
                b = j % 2
                act.wait_ge(turned, o * PAIRS + j + 1)
                need(act, proj_ok, o * PAIRS + j - 1)
                nc.scalar.activation(tT[0:D, b, :, :], ps_t[0:D, b, :, 0:3 * P], ACT.Copy).then_inc(t_ok, 1)

            def queries(o, j):
                b = j % 2
                act.wait_ge(proj_ok, o * PAIRS + j + 1)
                need(act, kq_ok, o * PAIRS + j - 1)
                nc.scalar.activation(qs[:, b, :, :], ps_p[:, b, :, 2 * D:3 * D], ACT.Copy,
                                     scale=float(HD) ** -0.5).then_inc(q_ok, 1)

            def scores(o, j):
                b = j % 2
                act.wait_ge(clip_ok, o * PAIRS + j + 1)
                need(act, head_ok, o * PAIRS + j - 1)
                nc.scalar.activation(msg[:, b, :, D:C], clip[:, b, :, :], ACT.Exp).then_inc(exp_ok, 1)

            def lap(o, last=False):
                for j in range(PAIRS):
                    if not (last and j + 1 >= PAIRS):
                        turn(*ahead(o, j, 1))
                    if not (last and j + 2 >= PAIRS):
                        spread(*ahead(o, j, 2))
                    queries(o, j)
                    scores(o, j)
                    if not (last and j + 2 >= PAIRS):
                        relu(*ahead(o, j, 2))

            act.wait_ge(prep, 1)
            for j in range(2):
                spread(0, j)
                relu(0, j)
            turn(0, 0)
            lap(0)
            with act.Fori(1, LAPS - 1) as o:
                lap(o)
            lap(LAPS - 1, last=True)

        @block.tensor
        def _(pe):
            def transposes(o, j):
                b = j % 2
                pe.wait_ge(h_ok, o * PAIRS + j + 1)
                if j % (PAIRS // 2) == 0:
                    pe.wait_ge(ea_in[2 * j // PAIRS], (o + 1) * 16)
                if isinstance(o, int) and o == LAPS - 1 and j == PAIRS - 1:
                    pe.wait_ge(rest_in, 16)
                need(pe, t_ok, o * PAIRS + j - 1)
                for k in range(2):
                    for part, what in enumerate((hb[:, b, k, :], hb[:, b, 2 + k, :], ea[:, 2 * j + k, :])):
                        last = nc.tensor.transpose(ps_t[0:D, b, k, part * P:(part + 1) * P], what, ident[:, :])
                last.then_inc(turned, 1)

            def project(o, j):
                b = j % 2
                pe.wait_ge(t_ok, o * PAIRS + j + 1)
                need(pe, msg_ok, o * PAIRS + j - 1)
                for k in range(2):
                    for part, lo, hi in ((0, 0, 2 * D), (1, 2 * D, 3 * D), (2, 3 * D, W4)):
                        last = nc.tensor.matmul(ps_p[:, b, k, lo:hi], tT[:, b, k, part * P:(part + 1) * P],
                                                w_all[:, lo:hi], start=True, stop=True)
                last.then_inc(proj_ok, 1)

            def lap(o, last=False):
                for j in range(PAIRS):
                    if not (last and j + 1 >= PAIRS):
                        transposes(*ahead(o, j, 1))
                        project(*ahead(o, j, 1))

            pe.wait_ge(made, 2)
            pe.wait_ge(viol_in, 1)
            nc.tensor.matmul(ps_p[:, 1, 1, 0:1], ones[:, :], viol[:, :], start=True, stop=True).then_inc(viol_sum, 1)
            pe.wait_ge(w_in, 128)
            pe.wait_ge(pre, 1)
            transposes(0, 0)
            project(0, 0)
            lap(0)
            with pe.Fori(1, LAPS - 1) as o:
                lap(o)
            lap(LAPS - 1, last=True)

            pe.wait_ge(rec_ids, 1)
            for g in range(3):
                last = nc.tensor.matmul(ps_t[:, 0, 0, g * P:(g + 1) * P], ones[:, :], diag[:, g, :],
                                        start=True, stop=True)
            last.then_inc(rec_b, 1)
            pe.wait_ge(rec_eq, 1)
            for g in range(3):
                for h in range(3):
                    nc.tensor.matmul(ps_p[:, 0, 0, g * C:(g + 1) * C], eq[:, h, g * P:(g + 1) * P], rmat[:, h, :],
                                     start=h == 0, stop=h == 2)
            for g in range(3):
                for h in range(g + 1):
                    lhs = eqb[:, g, :] if h == g else eq[:, h, g * P:(g + 1) * P]
                    last = nc.tensor.matmul(ps_p[:, 0, 1, g:g + 1], lhs, ones[:, 0:1], start=h == 0, stop=h == g)
            last.then_inc(rec_sum, 1)

            pe.wait_ge(flag, 1)
            unsorted = pe.value_load(bad[0:1, 0:1])
            with pe.If(unsorted != 0):
                pe.sem_inc(hot_free, 2)
                acc = ps_t[0:FN, 1, 0, 0:C]
                with pe.Fori(0, FTILES) as n:
                    pe.wait_ge(facc_free, n + 1)
                    nc.tensor.matmul(acc, ones[:, 0:FN], run[:, 0:C], start=True, stop=False)
                    with pe.Fori(0, TILES // (2 * FG)) as g:
                        for b in range(2):
                            pe.wait_ge(hot_ok, n * (TILES // FG) + g * 2 + b + 1)
                            for u in range(FG):
                                last = nc.tensor.matmul(
                                    acc, hot[b][:, u, :],
                                    run[:, bass.ds((g * (2 * FG) + (b * FG + u + 1)) * C, C)],
                                    start=False, stop=False)
                            last.then_inc(hot_free, 1)
                    nc.tensor.matmul(acc, ones[:, 0:FN], run[:, 0:C], start=False, stop=True).then_inc(facc_ok, 1)

        @block.vector
        def _(dve):
            V = nc.vector
            steps = [0]

            def step(ins):
                steps[0] += 1
                ins.then_inc(prep, 1)
                dve.wait_ge(prep, steps[0])

            V.memset(idx[:, :, COLS:TILES], 0)
            V.memset(nxt[:, COLS:TILES], SKIP).then_inc(blank, 1)
            V.memset(tT[D:D + 1, :, :, :], 1.0)
            V.memset(run[:, 0:C], 0.0)
            V.memset(head[:, :, :], 0.0)
            V.memset(put[:, COLS:TILES], SKIP)
            V.memset(goes_on[:, :], 0.0)
            V.memset(in_head[:, :], 0.0)
            step(V.memset(eps[:, :], EPS))

            def moments(o, j):
                b = j % 2
                dve.wait_ge(gathered[j], (o + 1) * 64)
                for k in range(4):
                    last = V.bn_stats(stats[:, b, k, :], (xs, xd)[k // 2][:, 2 * j + k % 2, :])
                last.then_inc(stat_s, 1)
                dve.wait_ge(stat_s, o * PAIRS + j + 1)
                dve.sem_inc(passed, 1)
                for k in range(4):
                    last = V.bn_aggr(mv[:, b, k, :], stats[:, b, k, :])
                last.then_inc(stat_ok, 1)

            def norms(o, j):
                b, n = j % 2, o * PAIRS + j + 1
                dve.wait_ge(rst0_ok, n)
                V.tensor_tensor(nwt[:, b, 0, :], rst0[:, b, :], rst0[:, b, :], ALU.mult).then_inc(nw0, 1)
                dve.wait_ge(nw0, n)
                V.scalar_tensor_tensor(nwt[:, b, 1, :], mv[:, b, :, 1], eps[:, :], nwt[:, b, 0, :],
                                       ALU.add, ALU.mult).then_inc(nw1, 1)
                dve.wait_ge(nw1, n)
                V.tensor_scalar(nwt[:, b, 0, :], nwt[:, b, 1, :], -0.5, 1.5, ALU.mult, ALU.add).then_inc(nw1b, 1)
                dve.wait_ge(nw1b, n)
                V.tensor_tensor(rstd[:, b, :], nwt[:, b, 0, :], rst0[:, b, :], ALU.mult).then_inc(rstd_ok, 1)
                dve.wait_ge(rstd_ok, n)
                V.scalar_tensor_tensor(nmr[:, b, :], mv[:, b, :, 0], -1.0, rstd[:, b, :],
                                       ALU.mult, ALU.mult).then_inc(norm_ok, 1)

            def products(o, j):
                b, n = j % 2, o * PAIRS + j + 1
                dve.wait_ge(q_ok, n)
                V.tensor_tensor(kq[:, b, :, :], ps_p[:, b, :, 0:D], qs[:, b, :, :], ALU.mult).then_inc(kq_ok, 1)
                dve.wait_ge(kq_ok, n)
                V.tensor_tensor(kqe[:, b, :, :], ps_p[:, b, :, 3 * D:W4], kq[:, b, :, :], ALU.mult).then_inc(kqe_ok, 1)
                dve.wait_ge(kqe_ok, n)
                V.tensor_reduce(ssum[:, b, :, :].rearrange("p k h -> p (k h)"),
                                kqe[:, b, :, :].rearrange("p k (h d) -> p (k h) d", d=HD),
                                AX, ALU.add).then_inc(sum_ok, 1)
                dve.wait_ge(sum_ok, n)
                V.tensor_scalar(clip[:, b, :, :], ssum[:, b, :, :], -5.0, 5.0, ALU.max, ALU.min).then_inc(clip_ok, 1)

            def by_head(a):
                return a.rearrange("p k (h d) -> p k h d", d=HD)

            def wide(a):
                return a.unsqueeze(3).to_broadcast([P, a.shape[1], H, HD])

            def sums(o, j):
                b, n = j % 2, o * PAIRS + j + 1
                dve.wait_ge(exp_ok, n)
                V.tensor_tensor(by_head(msg[:, b, :, 0:D]), by_head(ps_p[:, b, :, D:2 * D]),
                                wide(msg[:, b, :, D:C]), ALU.mult).then_inc(msg_ok, 1)
                dve.wait_ge(msg_ok, n)
                for k in range(2):
                    t = o * LAP + 2 * j + k
                    V.scalar_tensor_tensor(run[:, bass.ds((t + 1) * C, C)], run[:, bass.ds(t * C, C)],
                                           goes_on[:, bass.ds(t, 1)], msg[:, b, k, :],
                                           ALU.mult, ALU.add).then_inc((run0_ok, run1_ok)[k], 1)
                    V.scalar_tensor_tensor(head[:, k, :], msg[:, b, k, :], in_head[:, bass.ds(t, 1)],
                                           head[:, k, :], ALU.mult, ALU.add).then_inc((head0_ok, head_ok)[k], 1)
                    if k == 0:
                        dve.wait_ge(run0_ok, n)
                        need(dve, head_ok, n - 1)
                pair = run[:, bass.ds((o * LAP + 2 * j + 1) * C, 2 * C)].rearrange("p (k c) -> p k c", k=2)
                dve.wait_ge(run1_ok, n)
                V.tensor_scalar(zeps[:, b, :, :], pair[:, :, D:C], 1e-6, None, ALU.add).then_inc(zeps_ok, 1)
                dve.wait_ge(zeps_ok, n)
                V.reciprocal(zinv[:, b, :, :], zeps[:, b, :, :]).then_inc(zinv_ok, 1)
                dve.wait_ge(zinv_ok, n)
                V.tensor_tensor(by_head(hout[:, b, :, :]), by_head(pair[:, :, 0:D]), wide(zinv[:, b, :, :]),
                                ALU.mult).then_inc(hout_ok, 1)
                dve.wait_ge(hout_ok, n)
                need(dve, scattered[j], o * 32)
                V.tensor_tensor(rows[:, 2 * j:2 * j + 2, :], hout[:, b, :, :], xd[:, 2 * j:2 * j + 2, :],
                                ALU.add).then_inc(rows_ok, 1)

            def lap(o, last=False):
                for j in range(PAIRS):
                    more = not (last and j + 2 >= PAIRS)
                    if more:
                        moments(*ahead(o, j, 2))
                    products(o, j)
                    if more:
                        norms(*ahead(o, j, 2))
                    sums(o, j)

            dve.wait_ge(idx_in, 96)
            dve.wait_ge(made, 2)
            V.tensor_copy(dstf[:, :], idx[:, 1, :])
            V.tensor_copy(nxtf[:, :], nxt[:, :])
            V.tensor_copy(node[:, :], nodei[:, :])
            step(V.tensor_copy(pf[:, :], pi[:, :]))
            step(V.tensor_tensor(mask[:, :], dstf[:, :], nxtf[:, :], ALU.is_gt))
            V.tensor_reduce(viol[:, :], mask[:, :], AX, ALU.max).then_inc(viol_in, 1)
            V.tensor_scalar(neg[:, 0:1], pf[:, :], -1.0, -1.0, ALU.mult, ALU.add)
            V.tensor_scalar(neg[:, 2:3], pf[:, :], -1.0, -1.0 - P, ALU.mult, ALU.add)
            V.tensor_scalar(real[:, 1:2], pf[:, :], float(REST), None, ALU.is_lt)
            first, final = dstf[:, 0:1], dstf[:, COLS - 1:COLS]
            step(V.tensor_tensor(real[:, 0:1], first, final, ALU.not_equal))
            V.tensor_tensor(dif[:, 0:1], first, neg[:, 0:1], ALU.subtract)
            step(V.tensor_tensor(dif[:, 1:2], dstf[:, COLS:TILES], neg[:, 2:3], ALU.subtract))
            V.scalar_tensor_tensor(ids[:, 0:1], dif[:, 0:1], real[:, 0:1], neg[:, 0:1], ALU.mult, ALU.add)
            V.tensor_copy(ids[:, 1:2], final)
            step(V.scalar_tensor_tensor(ids[:, 2:3], dif[:, 1:2], real[:, 1:2], neg[:, 2:3], ALU.mult, ALU.add))
            step(V.tensor_copy(dstf[:, COLS:TILES], ids[:, 2:3]))
            dve.wait_ge(viol_sum, 1)
            V.tensor_copy(bad[:, :], ps_p[:, 1, 1, 0:1])
            step(V.tensor_scalar(sorted_[:, :], ps_p[:, 1, 1, 0:1], 0.0, None, ALU.is_equal))
            d = dstf[:, 0:COLS]
            step(V.tensor_tensor(mask[:, 0:COLS], d, nxtf[:, 0:COLS], ALU.not_equal))
            step(V.scalar_tensor_tensor(mask[:, 0:COLS], d, first, mask[:, 0:COLS], ALU.not_equal, ALU.mult))
            step(V.scalar_tensor_tensor(mask[:, 0:COLS], d, final, mask[:, 0:COLS], ALU.not_equal, ALU.mult))
            step(V.scalar_tensor_tensor(nxtf[:, 0:COLS], d, -float(SKIP), mask[:, 0:COLS], ALU.add, ALU.mult))
            V.tensor_scalar(put[:, 0:COLS], nxtf[:, 0:COLS], sorted_[:, :], float(SKIP), ALU.mult, ALU.add)
            step(V.tensor_tensor(mask[:, 1:COLS], dstf[:, 1:COLS], dstf[:, 0:COLS - 1], ALU.is_equal))
            V.tensor_scalar(goes_on[:, 1:COLS], mask[:, 1:COLS], sorted_[:, :], None, ALU.mult)
            V.tensor_scalar(in_head[:, 0:COLS], d, first, None, ALU.is_equal)
            step(V.tensor_copy(left[:, :], dstf[:, :]))
            V.memset(nwt[:, :, :, :], 0.0).then_inc(pre, 1)
            dve.wait_ge(pre, 1)

            for j in range(2):
                moments(0, j)
                norms(0, j)
            lap(0)
            with dve.Fori(1, LAPS - 1) as o:
                lap(o)
            lap(LAPS - 1, last=True)

            recs = [0]

            def rec(ins):
                recs[0] += 1
                ins.then_inc(rec_step, 1)
                dve.wait_ge(rec_step, recs[0])

            dve.wait_ge(head_ok, TILES // 2)
            V.tensor_tensor(rmat[:, 0, :], head[:, 0, :], head[:, 1, :], ALU.add)
            V.tensor_copy(rmat[:, 1, :], run[:, COLS * C:TILES * C])
            V.tensor_copy(rmat[:, 2, :], run[:, TILES * C:(TILES + 1) * C])
            for g in range(3):
                last = V.tensor_scalar(diag[:, g, :], ident[:, :], ids[:, g:g + 1], None, ALU.mult)
            last.then_inc(rec_ids, 1)
            dve.wait_ge(rec_b, 1)
            for h in range(3):
                last = V.tensor_scalar(eq[:, h, :], ps_t[:, 0, 0, 0:3 * P], ids[:, h:h + 1], None, ALU.is_equal)
            rec(last)
            for g in range(3):
                last = V.tensor_tensor(eqb[:, g, :], eq[:, g, g * P:(g + 1) * P], before[:, :], ALU.mult)
            last.then_inc(rec_eq, 1)
            dve.wait_ge(rec_sum, 1)
            sums3 = ps_p[:, 0, 0, 0:3 * C].rearrange("p (k c) -> p k c", k=3)
            rec(V.tensor_scalar(rz[:, 0, :, :], sums3[:, :, D:C], 1e-6, None, ALU.add))
            rec(V.reciprocal(rz[:, 1, :, :], rz[:, 0, :, :]))
            rec(V.tensor_tensor(by_head(rh[:, :, :]), by_head(sums3[:, :, 0:D]), wide(rz[:, 1, :, :]), ALU.mult))
            dve.wait_ge(rec_x, 48)
            V.tensor_tensor(rrow[:, :, :], rh[:, :, :], rx[:, :, :], ALU.add)
            V.tensor_scalar(rsel[:, 0, :], ps_p[:, 0, 1, 0:3], 0.0, None, ALU.is_equal)
            V.tensor_scalar(rsel[:, 1, :], ids[:, :], 0.0, sorted_[:, :], ALU.is_ge, ALU.mult)
            rec(V.tensor_scalar(rsel[:, 2, :], ids[:, :], -float(SKIP), None, ALU.add))
            rec(V.tensor_tensor(rsel[:, 0, :], rsel[:, 0, :], rsel[:, 1, :], ALU.mult))
            rec(V.tensor_tensor(rsel[:, 3, :], rsel[:, 0, :], rsel[:, 2, :], ALU.mult))
            V.tensor_scalar(rput[:, :], rsel[:, 3, :], float(SKIP), None, ALU.add).then_inc(rec_ok, 1)

            dve.sem_inc(flag, 1)
            unsorted = dve.value_load(bad[0:1, 0:1])
            with dve.If(unsorted != 0):
                V.memset(fz[:, :, :], 0.0).then_inc(facc_free, 1)
                GROUPS = TILES // FG
                with dve.Fori(0, FTILES) as n:
                    with dve.Fori(0, GROUPS // 2) as g:
                        for b in range(2):
                            dve.wait_ge(hot_free, n * GROUPS + g * 2 + b + 1)
                            V.tensor_tensor(
                                hot[b][:, :, :],
                                node[:, :].unsqueeze(1).to_broadcast([P, FG, FN]),
                                left[:, bass.ds(g * (2 * FG) + b * FG, FG)].unsqueeze(2).to_broadcast([P, FG, FN]),
                                ALU.is_equal).then_inc(hot_ok, 1)
                    dve.wait_ge(facc_ok, n + 1)
                    V.tensor_scalar(left[:, :], left[:, :], -float(FN), None, ALU.add)
                    acc = ps_t[0:FN, 1, 0, 0:C]
                    V.tensor_scalar(fz[:, 0, :], acc[:, D:C], 1e-6, None, ALU.add).then_inc(f_step, 1)
                    dve.wait_ge(f_step, n * 3 + 1)
                    V.reciprocal(fz[:, 1, :], fz[:, 0, :]).then_inc(f_step, 1)
                    dve.wait_ge(f_step, n * 3 + 2)
                    V.tensor_tensor(fh[:, :].rearrange("p (h d) -> p h d", d=HD),
                                    acc[:, 0:D].rearrange("p (h d) -> p h d", d=HD),
                                    fz[:, 1, :].unsqueeze(2).to_broadcast([FN, H, HD]),
                                    ALU.mult).then_inc(facc_free, 1)
                    dve.wait_ge(facc_free, n + 2)
                    dve.wait_ge(fx_in, (n + 1) * 16)
                    V.tensor_tensor(fo[:, :], fh[:, :], fx[:, :], ALU.add).then_inc(fo_ok, 1)
                    V.memset(fz[:, 0, :], 0.0).then_inc(f_step, 1)


_INS = ["x", "src", "dst", "edge_attr_96", "L0_gnn_Wq", "L0_gnn_bq", "L0_gnn_Wk", "L0_gnn_bk",
        "L0_gnn_We", "L0_gnn_be", "L0_gnn_Wv", "L0_gnn_bv"]


def kernel(**inputs):
    import numpy as _np
    import concourse.bacc as _bacc
    from concourse import mybir as _mybir
    from concourse.bass_utils import run_bass_kernel_spmd as _run

    nc = _bacc.Bacc("TRN2", target_bir_lowering=False, num_devices=1)
    arrays, args = {}, []
    for name in _INS:
        a = _np.ascontiguousarray(inputs[name])
        arrays[f"in_{name}_dram"] = a
        args.append(nc.dram_tensor(f"in_{name}_dram", a.shape, _mybir.dt.from_np(a.dtype), kind="ExternalInput").ap())
    shape = inputs["x"].shape
    out = nc.dram_tensor("out_dram", shape, _mybir.dt.float32, kind="ExternalOutput").ap()
    gnn_edge_attention(nc, *args, out)
    r = _run(nc, [arrays], core_ids=[0])
    return r.results[0]["out_dram"]
```

```python
import concourse.bass as bass
from concourse import mybir
from contextlib import ExitStack


def gnn_edge_attention(nc, x, src, dst, edge_attr, wq, bq, wk, bk, we, be, wv, bv, out):
    f32 = mybir.dt.float32
    i32 = mybir.dt.int32
    ALU = mybir.AluOpType
    ACT = mybir.ActivationFunctionType
    AX = mybir.AxisListType.X

    P = 128
    N, D = x.shape
    E = src.shape[0]
    H = 8
    HD = D // H
    C = D + H
    COLS = E // P
    REST = E - P * COLS
    TILES = COLS + 1
    PAIRS = 14
    LAP = 2 * PAIRS
    HALF = LAP // 2
    LAPS = TILES // LAP
    SKIP = 1 << 20
    EPS = 1e-5
    assert TILES == LAPS * LAP and REST > 0 and D == H * HD
    W4 = 4 * D
    CHUNKS = 15
    FN = 125
    FG = 14
    FTILES = N // FN
    assert N % FN == 0 and TILES % (2 * FG) == 0

    ctx = ExitStack()
    with ctx:
        def sb(name, shape, dt=f32):
            return ctx.enter_context(nc.sbuf_tensor(name, shape, dt))

        def sem(name):
            return ctx.enter_context(nc.semaphore(name))

        idx = sb("idx", [P, 2, TILES], i32)
        nxt = sb("nxt", [P, TILES], i32)
        put = sb("put", [P, TILES], i32)
        dstf = sb("dstf", [P, TILES])
        nxtf = sb("nxtf", [P, TILES])
        mask = sb("mask", [P, TILES])
        goes_on = sb("goes_on", [P, TILES])
        in_head = sb("in_head", [P, TILES])
        take = [sb(f"take{b}", [P, 2, LAP], i32) for b in range(2)]
        give = [sb(f"give{b}", [P, LAP], i32) for b in range(2)]
        xs = sb("xs", [P, LAP, D])
        xd = sb("xd", [P, LAP, D])
        ea = sb("ea", [P, LAP, D])
        rows = sb("rows", [P, 2 * LAP, D])
        stats = sb("stats", [P, 2, 4, 6])
        mv = sb("mv", [P, 2, 4, 2])
        lnv = sb("lnv", [P, 2, 4])
        rst0 = sb("rst0", [P, 2, 4])
        nwt = sb("nwt", [P, 2, 2, 4])
        rstd = sb("rstd", [P, 2, 4])
        nmr = sb("nmr", [P, 2, 4])
        hb = sb("hb", [P, 2, 4, D])
        tT = sb("tT", [D + 1, 2, 2, 3 * P])
        qs = sb("qs", [P, 2, 2, D])
        kq = sb("kq", [P, 2, 2, D])
        kqe = sb("kqe", [P, 2, 2, D])
        ssum = sb("ssum", [P, 2, 2, H])
        clip = sb("clip", [P, 2, 2, H])
        msg = sb("msg", [P, 2, 2, C])
        zeps = sb("zeps", [P, 2, 2, H])
        zinv = sb("zinv", [P, 2, 2, H])
        hout = sb("hout", [P, 2, 2, D])
        run = sb("run", [P, (TILES + 1) * C])
        head = sb("head", [P, 2, C])
        w_all = sb("w_all", [D + 1, W4])
        ident = sb("ident", [P, P])
        ones = sb("ones", [P, P])
        before = sb("before", [P, P])
        eps = sb("eps", [P, 1])
        pi = sb("pi", [P, 1], i32)
        pf = sb("pf", [P, 1])
        neg = sb("neg", [P, 3])
        real = sb("real", [P, 2])
        dif = sb("dif", [P, 2])
        viol = sb("viol", [P, 1])
        bad = sb("bad", [P, 1], i32)
        sorted_ = sb("sorted_", [P, 1])
        ids = sb("ids", [P, 3])
        diag = sb("diag", [P, 3, P])
        eq = sb("eq", [P, 3, 3 * P])
        eqb = sb("eqb", [P, 3, P])
        rmat = sb("rmat", [P, 3, C])
        rx = sb("rx", [P, D])
        rz = sb("rz", [P, 2, 3, H])
        rh = sb("rh", [P, 3, D])
        rrow = sb("rrow", [P, 3, D])
        rsel = sb("rsel", [P, 4, 3])
        rput = sb("rput", [P, 3], i32)
        nodei = sb("nodei", [P, FN], i32)
        node = sb("node", [P, FN])
        left = sb("left", [P, TILES])
        hot = [sb(f"hot{b}", [P, FG, FN]) for b in range(2)]
        fx = sb("fx", [FN, D])
        fz = sb("fz", [FN, 2, H])
        fh = sb("fh", [FN, D])
        fo = sb("fo", [FN, D])

        ps_t = ctx.enter_context(nc.psum_tensor("ps_t", [P, 2, 2, 512], f32))
        ps_p = ctx.enter_context(nc.psum_tensor("ps_p", [P, 2, 2, 512], f32))

        blank = sem("blank")
        idx_in = sem("idx_in")
        side_in = sem("side_in")
        w_in = sem("w_in")
        copied = sem("copied")
        ea_in = [sem(f"ea_in{h}") for h in range(2)]
        rest_in = sem("rest_in")
        gathered = [sem(f"gathered{j}") for j in range(PAIRS)]
        scattered = [sem(f"scattered{j}") for j in range(PAIRS)]
        kept = sem("kept")
        taken = sem("taken")
        staged = sem("staged")
        made = sem("made")
        prep = sem("prep")
        pre = sem("pre")
        viol_in = sem("viol_in")
        viol_sum = sem("viol_sum")
        stat_s = sem("stat_s")
        stat_ok = sem("stat_ok")
        passed = sem("passed")
        ln_ok = sem("ln_ok")
        rst0_ok = sem("rst0_ok")
        nw0 = sem("nw0")
        nw1 = sem("nw1")
        rstd_ok = sem("rstd_ok")
        norm_ok = sem("norm_ok")
        h_ok = sem("h_ok")
        turned = sem("turned")
        t_ok = sem("t_ok")
        proj_ok = sem("proj_ok")
        q_ok = sem("q_ok")
        kq_ok = sem("kq_ok")
        kqe_ok = sem("kqe_ok")
        sum_ok = sem("sum_ok")
        clip_ok = sem("clip_ok")
        exp_ok = sem("exp_ok")
        msg_ok = sem("msg_ok")
        run0_ok = sem("run0_ok")
        run1_ok = sem("run1_ok")
        head0_ok = sem("head0_ok")
        head_ok = sem("head_ok")
        zeps_ok = sem("zeps_ok")
        zinv_ok = sem("zinv_ok")
        hout_ok = sem("hout_ok")
        rows_ok = sem("rows_ok")
        rec_ids = sem("rec_ids")
        rec_b = sem("rec_b")
        rec_eq = sem("rec_eq")
        rec_sum = sem("rec_sum")
        rec_step = sem("rec_step")
        rec_ok = sem("rec_ok")
        rec_out = sem("rec_out")
        flag = sem("flag")
        hot_ok = sem("hot_ok")
        hot_free = sem("hot_free")
        facc_ok = sem("facc_ok")
        facc_free = sem("facc_free")
        f_step = sem("f_step")
        fx_in = sem("fx_in")
        fo_ok = sem("fo_ok")
        fo_out = sem("fo_out")

        block = ctx.enter_context(nc.Block())

        def need(eng, s, value):
            if not isinstance(value, int) or value > 0:
                eng.wait_ge(s, value)

        def off(o, j, by):
            o, j = o + (j + by) // PAIRS if (j + by) // PAIRS else o, (j + by) % PAIRS
            return None if isinstance(o, int) and not 0 <= o < LAPS else (o, j)

        def at(stage, pair):
            if pair is not None:
                stage(*pair)

        @block.sync
        def _(sp):
            def columns(a, lo=0):
                return a[lo:lo + P * COLS].rearrange("(p t) -> p t", p=P)

            sp.dma_start(idx[:, 0, 0:COLS], columns(src)).then_inc(idx_in, 16)
            sp.dma_start(idx[:, 1, 0:COLS], columns(dst)).then_inc(idx_in, 16)
            sp.dma_start(nxt[:, 0:COLS], columns(dst, 1)).then_inc(side_in, 16)
            sp.wait_ge(blank, 1)
            sp.dma_start(idx[0:REST, 0, COLS:TILES], src[P * COLS:E].unsqueeze(1)).then_inc(side_in, 16)
            sp.dma_start(idx[0:REST, 1, COLS:TILES], dst[P * COLS:E].unsqueeze(1)).then_inc(side_in, 16)
            sp.dma_start(nxt[0:REST - 1, COLS:TILES], dst[P * COLS + 1:E].unsqueeze(1)).then_inc(side_in, 16)
            for k, (w, b) in enumerate(((wk, bk), (wv, bv), (wq, bq), (we, be))):
                sp.dma_start(w_all[0:D, k * D:(k + 1) * D], w[:, :]).then_inc(w_in, 16)
                sp.dma_start(w_all[D:D + 1, k * D:(k + 1) * D], b[:].unsqueeze(0)).then_inc(w_in, 16)

            table = edge_attr[0:P * COLS, :].rearrange("(p t) d -> p t d", p=P)

            def load(o, last=False):
                for h in range(2):
                    need(sp, turned, (o - 1) * PAIRS + (h + 1) * PAIRS // 2)
                    n = HALF - 1 if last and h == 1 else HALF
                    sp.dma_start(ea[:, h * HALF:h * HALF + n, :],
                                 table[:, bass.ds(o * LAP + h * HALF, n), :]).then_inc(ea_in[h], 16)
                    if n < HALF:
                        sp.dma_start(ea[0:REST, LAP - 1, :], edge_attr[P * COLS:E, :]).then_inc(rest_in, 16)

            load(0)
            xc = x.rearrange("n d -> (n d)").rearrange("(c p f) -> c p f", c=CHUNKS, p=P)
            oc = out.rearrange("n d -> (n d)").rearrange("(c p f) -> c p f", c=CHUNKS, p=P)
            for c in range(CHUNKS):
                if c > 1:
                    sp.wait_ge(gathered[c - 2], 64)
                sp.dma_start(oc[c, :, :], xc[c, :, :], max_dma_last_dim=4096).then_inc(copied, 16)
            with sp.Fori(1, LAPS - 1) as o:
                load(o)
            load(LAPS - 1, last=True)

            sp.wait_ge(flag, 1)
            unsorted = sp.value_load(bad[0:1, 0:1])
            with sp.If(unsorted != 0):
                sp.wait_ge(copied, 16 * CHUNKS)
                sp.sem_inc(fo_out, 16)
                with sp.Fori(0, FTILES) as n:
                    sp.wait_ge(fo_out, (n + 1) * 16)
                    sp.dma_start(fx[:, :], x[bass.ds(n * FN, FN), :]).then_inc(fx_in, 16)
                    sp.wait_ge(fo_ok, n + 1)
                    sp.dma_start(out[bass.ds(n * FN, FN), :], fo[:, :]).then_inc(fo_out, 16)
                sp.wait_ge(fo_out, (FTILES + 1) * 16)
            sp.wait_ge(copied, 16 * CHUNKS)
            for j in range(PAIRS):
                sp.wait_ge(scattered[j], 32 * LAPS - (16 if j == PAIRS - 1 else 0))
            sp.wait_ge(rec_out, 48)

        @block.gpsimd
        def _(pool):
            nc.gpsimd.iota(pi[:, :], [[1, 1]], base=0, channel_multiplier=1)
            nc.gpsimd.iota(nodei[:, :], [[1, FN]], base=0, channel_multiplier=0)
            nc.gpsimd.memset(ones[:, :], 1.0)
            nc.gpsimd.memset(ident[:, :], 0.0)
            nc.gpsimd.memset(before[:, :], 1.0).then_inc(made, 1)
            pool.wait_ge(made, 1)
            nc.gpsimd.affine_select(out=ident[:, :], in_=ident[:, :], compare_op=ALU.not_equal, fill=1.0, base=0,
                                    pattern=[[-1, P]], channel_multiplier=1)
            nc.gpsimd.affine_select(out=before[:, :], in_=before[:, :], compare_op=ALU.is_gt, fill=0.0, base=0,
                                    pattern=[[1, P]], channel_multiplier=-1).then_inc(made, 1)

            def stage(o, odd):
                nc.gpsimd.tensor_copy(take[odd][:, :, :], idx[:, :, bass.ds(o * LAP, LAP)])
                nc.gpsimd.tensor_copy(give[odd][:, :], put[:, bass.ds((o - 2) * LAP, LAP)]).then_inc(staged, 1)
                pool.wait_ge(staged, o - 1)
                pool.sem_inc(taken, 1)

            def numbers(o, odd, side, t):
                if isinstance(o, int):
                    return (idx[:, side, o * LAP + t:o * LAP + t + 1] if side < 2
                            else put[:, (o - 2) * LAP + t:(o - 2) * LAP + t + 1])
                return take[odd][:, side, t:t + 1] if side < 2 else give[odd][:, t:t + 1]

            def lap(o, odd, gather=True, scatter=True):
                if not isinstance(o, int):
                    stage(o, odd)
                for j in range(PAIRS):
                    if gather and (not isinstance(o, int) or o > 0):
                        pool.wait_ge(rows_ok, (o - 1) * PAIRS + j + 1)
                        pool.sem_inc(taken, 1)
                    if scatter and not gather:
                        pool.wait_ge(rows_ok, (o - 2) * PAIRS + j + 1)
                        pool.sem_inc(taken, 1)
                    for t in (2 * j, 2 * j + 1):
                        if scatter and not (isinstance(o, int) and (o - 2) * LAP + t == COLS):
                            nc.gpsimd.indirect_dma_start(
                                out[:, :], bass.IndirectOffsetOnAxis(ap=numbers(o, odd, 2, t), axis=0),
                                rows[:, odd * LAP + t, :], None, bounds_check=N - 1, oob_is_err=False,
                            ).then_inc(scattered[j], 16)
                        if gather:
                            for side, into in ((0, xs), (1, xd)):
                                nc.gpsimd.indirect_dma_start(
                                    into[:, t, :], None, x[:, :],
                                    bass.IndirectOffsetOnAxis(ap=numbers(o, odd, side, t), axis=0),
                                ).then_inc(gathered[j], 16)

            pool.wait_ge(idx_in, 32)
            lap(0, 0, scatter=False)
            lap(1, 1, scatter=False)
            pool.wait_ge(copied, 16 * CHUNKS)
            pool.wait_ge(pre, 1)
            pool.sem_inc(taken, 1)
            with pool.Fori(2, LAPS - 1, 2) as o:
                lap(o, 0)
                lap(o + 1, 1)
            lap(LAPS - 1, 0)
            lap(LAPS, 1, gather=False)
            lap(LAPS + 1, 0, gather=False)
            pool.wait_ge(rec_ok, 1)
            for g in range(3):
                nc.gpsimd.indirect_dma_start(
                    out[:, :], bass.IndirectOffsetOnAxis(ap=rput[:, g:g + 1], axis=0),
                    rrow[:, g, :], None, bounds_check=N - 1, oob_is_err=False).then_inc(rec_out, 16)

        @block.scalar
        def _(act):
            def spread(o, j):
                b = j % 2
                act.wait_ge(stat_ok, o * PAIRS + j + 1)
                nc.scalar.activation(lnv[:, b, :], mv[:, b, :, 1], ACT.Ln, bias=eps[:, :]).then_inc(ln_ok, 1)
                act.wait_ge(ln_ok, o * PAIRS + j + 1)
                nc.scalar.activation(rst0[:, b, :], lnv[:, b, :], ACT.Exp, scale=-0.5).then_inc(rst0_ok, 1)

            def relu(o, j):
                b = j % 2
                act.wait_ge(norm_ok, o * PAIRS + j + 1)
                need(act, turned, o * PAIRS + j - 1)
                for k in range(4):
                    part = (xs, xd)[k // 2][:, 2 * j + k % 2, :]
                    last = nc.scalar.activation(hb[:, b, k, :], part, ACT.Relu, bias=nmr[:, b, k:k + 1],
                                                scale=rstd[:, b, k:k + 1])
                last.then_inc(h_ok, 1)

            def turn(o, j):
                b = j % 2
                act.wait_ge(turned, o * PAIRS + j + 1)
                need(act, proj_ok, o * PAIRS + j - 1)
                nc.scalar.activation(tT[0:D, b, :, :], ps_t[0:D, b, :, 0:3 * P], ACT.Copy).then_inc(t_ok, 1)

            def queries(o, j):
                b = j % 2
                act.wait_ge(proj_ok, o * PAIRS + j + 1)
                need(act, kq_ok, o * PAIRS + j - 1)
                nc.scalar.activation(qs[:, b, :, :], ps_p[:, b, :, 2 * D:3 * D], ACT.Copy,
                                     scale=float(HD) ** -0.5).then_inc(q_ok, 1)

            def scores(o, j):
                b = j % 2
                act.wait_ge(clip_ok, o * PAIRS + j + 1)
                need(act, head_ok, o * PAIRS + j - 1)
                nc.scalar.activation(msg[:, b, :, D:C], clip[:, b, :, :], ACT.Exp).then_inc(exp_ok, 1)

            def lap(o):
                for j in range(PAIRS):
                    queries(o, j)
                    at(turn, off(o, j, 1))
                    scores(o, j)
                    at(relu, off(o, j, 2))
                    at(spread, off(o, j, 3))

            nc.scalar.preload_act_table_set("natural_log_exp_and_others")
            act.wait_ge(prep, 1)
            for j in range(2):
                spread(0, j)
                relu(0, j)
            turn(0, 0)
            spread(0, 2)
            lap(0)
            with act.Fori(1, LAPS - 1) as o:
                lap(o)
            lap(LAPS - 1)

        @block.tensor
        def _(pe):
            def transposes(o, j):
                b = j % 2
                pe.wait_ge(h_ok, o * PAIRS + j + 1)
                if j % (PAIRS // 2) == 0:
                    pe.wait_ge(ea_in[2 * j // PAIRS], (o + 1) * 16)
                if isinstance(o, int) and o == LAPS - 1 and j == PAIRS - 1:
                    pe.wait_ge(rest_in, 16)
                need(pe, t_ok, o * PAIRS + j - 1)
                for k in range(2):
                    for part, what in enumerate((hb[:, b, k, :], hb[:, b, 2 + k, :], ea[:, 2 * j + k, :])):
                        last = nc.tensor.transpose(ps_t[0:D, b, k, part * P:(part + 1) * P], what, ident[:, :])
                last.then_inc(turned, 1)

            def project(o, j):
                b = j % 2
                pe.wait_ge(t_ok, o * PAIRS + j + 1)
                need(pe, msg_ok, o * PAIRS + j - 1)
                for k in range(2):
                    for part, lo, hi in ((0, 0, 2 * D), (1, 2 * D, 3 * D), (2, 3 * D, W4)):
                        last = nc.tensor.matmul(ps_p[:, b, k, lo:hi], tT[:, b, k, part * P:(part + 1) * P],
                                                w_all[:, lo:hi], start=True, stop=True)
                last.then_inc(proj_ok, 1)

            def lap(o):
                for j in range(PAIRS):
                    at(transposes, off(o, j, 1))
                    at(project, off(o, j, 1))

            pe.wait_ge(made, 2)
            pe.wait_ge(viol_in, 1)
            nc.tensor.matmul(ps_p[:, 1, 1, 0:1], ones[:, :], viol[:, :], start=True, stop=True).then_inc(viol_sum, 1)
            pe.wait_ge(w_in, 128)
            pe.wait_ge(pre, 1)
            transposes(0, 0)
            project(0, 0)
            lap(0)
            with pe.Fori(1, LAPS - 1) as o:
                lap(o)
            lap(LAPS - 1)

            pe.wait_ge(rec_ids, 1)
            for g in range(3):
                last = nc.tensor.matmul(ps_t[:, 0, 0, g * P:(g + 1) * P], ones[:, :], diag[:, g, :],
                                        start=True, stop=True)
            last.then_inc(rec_b, 1)
            pe.wait_ge(rec_eq, 1)
            for g in range(3):
                for h in range(3):
                    nc.tensor.matmul(ps_p[:, 0, 0, g * C:(g + 1) * C], eq[:, h, g * P:(g + 1) * P], rmat[:, h, :],
                                     start=h == 0, stop=h == 2)
            for g in range(3):
                for h in range(g + 1):
                    lhs = eqb[:, g, :] if h == g else eq[:, h, g * P:(g + 1) * P]
                    last = nc.tensor.matmul(ps_p[:, 0, 1, g:g + 1], lhs, ones[:, 0:1], start=h == 0, stop=h == g)
            last.then_inc(rec_sum, 1)

            pe.wait_ge(flag, 1)
            unsorted = pe.value_load(bad[0:1, 0:1])
            with pe.If(unsorted != 0):
                pe.sem_inc(hot_free, 2)
                acc = ps_t[0:FN, 1, 0, 0:C]
                with pe.Fori(0, FTILES) as n:
                    pe.wait_ge(facc_free, n + 1)
                    nc.tensor.matmul(acc, ones[:, 0:FN], run[:, 0:C], start=True, stop=False)
                    with pe.Fori(0, TILES // (2 * FG)) as g:
                        for b in range(2):
                            pe.wait_ge(hot_ok, n * (TILES // FG) + g * 2 + b + 1)
                            for u in range(FG):
                                last = nc.tensor.matmul(
                                    acc, hot[b][:, u, :],
                                    run[:, bass.ds((g * (2 * FG) + (b * FG + u + 1)) * C, C)],
                                    start=False, stop=False)
                            last.then_inc(hot_free, 1)
                    nc.tensor.matmul(acc, ones[:, 0:FN], run[:, 0:C], start=False, stop=True).then_inc(facc_ok, 1)

        @block.vector
        def _(dve):
            V = nc.vector
            steps = [0]

            def step(ins):
                steps[0] += 1
                ins.then_inc(prep, 1)
                dve.wait_ge(prep, steps[0])

            V.memset(idx[:, :, COLS:TILES], 0)
            V.memset(nxt[:, COLS:TILES], SKIP).then_inc(blank, 1)
            V.memset(tT[D:D + 1, :, :, :], 1.0)
            V.memset(run[:, 0:C], 0.0)
            V.memset(head[:, :, :], 0.0)
            V.memset(put[:, COLS:TILES], SKIP)
            V.memset(goes_on[:, :], 0.0)
            V.memset(in_head[:, :], 0.0)
            step(V.memset(eps[:, :], EPS))

            def by_head(a):
                return a.rearrange("p k (h d) -> p k h d", d=HD)

            def wide(a):
                return a.unsqueeze(3).to_broadcast([P, a.shape[1], H, HD])

            def pair_of(o, j):
                return run[:, bass.ds((o * LAP + 2 * j + 1) * C, 2 * C)].rearrange("p (k c) -> p k c", k=2)

            def moments(o, j, half):
                b = j % 2
                if half == 0:
                    dve.wait_ge(gathered[j], (o + 1) * 64)
                part = (xs, xd)[half]
                V.bn_stats(stats[:, b, 2 * half, :], part[:, 2 * j, :])
                last = V.bn_stats(stats[:, b, 2 * half + 1, :], part[:, 2 * j + 1, :])
                if half == 1:
                    last.then_inc(stat_s, 1)

            def spreads(o, j):
                b = j % 2
                dve.wait_ge(stat_s, o * PAIRS + j + 1)
                dve.sem_inc(passed, 1)
                for k in range(4):
                    last = V.bn_aggr(mv[:, b, k, :], stats[:, b, k, :])
                last.then_inc(stat_ok, 1)

            def newton0(o, j):
                b = j % 2
                dve.wait_ge(rst0_ok, o * PAIRS + j + 1)
                V.scalar_tensor_tensor(nwt[:, b, 0, :], mv[:, b, :, 1], eps[:, :], rst0[:, b, :],
                                       ALU.add, ALU.mult).then_inc(nw0, 1)

            def newton1(o, j):
                b = j % 2
                dve.wait_ge(nw0, o * PAIRS + j + 1)
                V.scalar_tensor_tensor(nwt[:, b, 1, :], nwt[:, b, 0, :], -0.5, rst0[:, b, :],
                                       ALU.mult, ALU.mult).then_inc(nw1, 1)

            def newton2(o, j):
                b = j % 2
                dve.wait_ge(nw1, o * PAIRS + j + 1)
                V.scalar_tensor_tensor(rstd[:, b, :], nwt[:, b, 1, :], 1.5, rst0[:, b, :],
                                       ALU.add, ALU.mult).then_inc(rstd_ok, 1)

            def shifts(o, j):
                b = j % 2
                dve.wait_ge(rstd_ok, o * PAIRS + j + 1)
                V.scalar_tensor_tensor(nmr[:, b, :], mv[:, b, :, 0], -1.0, rstd[:, b, :],
                                       ALU.mult, ALU.mult).then_inc(norm_ok, 1)

            def times_q(o, j):
                b = j % 2
                dve.wait_ge(q_ok, o * PAIRS + j + 1)
                V.tensor_tensor(kq[:, b, :, :], ps_p[:, b, :, 0:D], qs[:, b, :, :], ALU.mult).then_inc(kq_ok, 1)

            def times_e(o, j):
                b = j % 2
                dve.wait_ge(kq_ok, o * PAIRS + j + 1)
                V.tensor_tensor(kqe[:, b, :, :], ps_p[:, b, :, 3 * D:W4], kq[:, b, :, :], ALU.mult).then_inc(kqe_ok, 1)

            def head_sums(o, j):
                b = j % 2
                dve.wait_ge(kqe_ok, o * PAIRS + j + 1)
                V.tensor_reduce(ssum[:, b, :, :].rearrange("p k h -> p (k h)"),
                                kqe[:, b, :, :].rearrange("p k (h d) -> p (k h) d", d=HD),
                                AX, ALU.add).then_inc(sum_ok, 1)

            def clips(o, j):
                b = j % 2
                dve.wait_ge(sum_ok, o * PAIRS + j + 1)
                V.tensor_scalar(clip[:, b, :, :], ssum[:, b, :, :], -5.0, 5.0, ALU.max, ALU.min).then_inc(clip_ok, 1)

            def messages(o, j):
                b = j % 2
                dve.wait_ge(exp_ok, o * PAIRS + j + 1)
                V.tensor_tensor(by_head(msg[:, b, :, 0:D]), by_head(ps_p[:, b, :, D:2 * D]),
                                wide(msg[:, b, :, D:C]), ALU.mult).then_inc(msg_ok, 1)

            def runs(o, j, k):
                t = o * LAP + 2 * j + k
                dve.wait_ge((msg_ok, run0_ok)[k], o * PAIRS + j + 1)
                V.scalar_tensor_tensor(run[:, bass.ds((t + 1) * C, C)], run[:, bass.ds(t * C, C)],
                                       goes_on[:, bass.ds(t, 1)], msg[:, j % 2, k, :],
                                       ALU.mult, ALU.add).then_inc((run0_ok, run1_ok)[k], 1)

            def heads(o, j, k):
                t = o * LAP + 2 * j + k
                V.scalar_tensor_tensor(head[:, k, :], msg[:, j % 2, k, :], in_head[:, bass.ds(t, 1)],
                                       head[:, k, :], ALU.mult, ALU.add).then_inc((head0_ok, head_ok)[k], 1)

            def z_up(o, j):
                b = j % 2
                dve.wait_ge(run1_ok, o * PAIRS + j + 1)
                V.tensor_scalar(zeps[:, b, :, :], pair_of(o, j)[:, :, D:C], 1e-6, None, ALU.add).then_inc(zeps_ok, 1)

            def z_inverse(o, j):
                b = j % 2
                dve.wait_ge(zeps_ok, o * PAIRS + j + 1)
                V.reciprocal(zinv[:, b, :, :], zeps[:, b, :, :]).then_inc(zinv_ok, 1)

            def means(o, j):
                b = j % 2
                dve.wait_ge(zinv_ok, o * PAIRS + j + 1)
                V.tensor_tensor(by_head(hout[:, b, :, :]), by_head(pair_of(o, j)[:, :, 0:D]),
                                wide(zinv[:, b, :, :]), ALU.mult).then_inc(hout_ok, 1)

            def finish(o, j):
                b = j % 2
                dve.wait_ge(hout_ok, o * PAIRS + j + 1)
                need(dve, scattered[j], (o - 1) * 32)
                V.tensor_tensor(rows[:, bass.ds(o % 2 * LAP + 2 * j, 2), :], hout[:, b, :, :], xd[:, 2 * j:2 * j + 2, :],
                                ALU.add).then_inc(rows_ok, 1)

            def work(o, j):
                here, back, on, far = (off(o, j, by) for by in (0, -1, 2, 3))
                at(times_q, here)
                at(messages, back)
                at(newton0, on)
                at(times_e, here)
                at(lambda *p: runs(*p, 0), back)
                at(newton1, on)
                at(head_sums, here)
                at(lambda *p: heads(*p, 0), back)
                at(newton2, on)
                at(clips, here)
                at(lambda *p: runs(*p, 1), back)
                at(shifts, on)
                at(lambda *p: heads(*p, 1), back)
                at(z_up, back)
                at(lambda *p: moments(*p, 0), far)
                at(z_inverse, back)
                at(lambda *p: moments(*p, 1), far)
                at(means, back)
                at(spreads, far)
                at(finish, back)

            def lap(o):
                for j in range(PAIRS):
                    work(o, j)

            dve.wait_ge(idx_in, 32)
            dve.wait_ge(side_in, 64)
            dve.wait_ge(made, 2)
            V.tensor_copy(dstf[:, :], idx[:, 1, :])
            V.tensor_copy(nxtf[:, :], nxt[:, :])
            V.tensor_copy(node[:, :], nodei[:, :])
            step(V.tensor_copy(pf[:, :], pi[:, :]))
            step(V.tensor_tensor(mask[:, :], dstf[:, :], nxtf[:, :], ALU.is_gt))
            V.tensor_reduce(viol[:, :], mask[:, :], AX, ALU.max).then_inc(viol_in, 1)
            V.tensor_scalar(neg[:, 0:1], pf[:, :], -1.0, -1.0, ALU.mult, ALU.add)
            V.tensor_scalar(neg[:, 2:3], pf[:, :], -1.0, -1.0 - P, ALU.mult, ALU.add)
            V.tensor_scalar(real[:, 1:2], pf[:, :], float(REST), None, ALU.is_lt)
            first, final = dstf[:, 0:1], dstf[:, COLS - 1:COLS]
            step(V.tensor_tensor(real[:, 0:1], first, final, ALU.not_equal))
            V.tensor_tensor(dif[:, 0:1], first, neg[:, 0:1], ALU.subtract)
            step(V.tensor_tensor(dif[:, 1:2], dstf[:, COLS:TILES], neg[:, 2:3], ALU.subtract))
            V.scalar_tensor_tensor(ids[:, 0:1], dif[:, 0:1], real[:, 0:1], neg[:, 0:1], ALU.mult, ALU.add)
            V.tensor_copy(ids[:, 1:2], final)
            step(V.scalar_tensor_tensor(ids[:, 2:3], dif[:, 1:2], real[:, 1:2], neg[:, 2:3], ALU.mult, ALU.add))
            step(V.tensor_copy(dstf[:, COLS:TILES], ids[:, 2:3]))
            dve.wait_ge(viol_sum, 1)
            V.tensor_copy(bad[:, :], ps_p[:, 1, 1, 0:1])
            step(V.tensor_scalar(sorted_[:, :], ps_p[:, 1, 1, 0:1], 0.0, None, ALU.is_equal))
            d = dstf[:, 0:COLS]
            step(V.tensor_tensor(mask[:, 0:COLS], d, nxtf[:, 0:COLS], ALU.not_equal))
            step(V.scalar_tensor_tensor(mask[:, 0:COLS], d, first, mask[:, 0:COLS], ALU.not_equal, ALU.mult))
            step(V.scalar_tensor_tensor(mask[:, 0:COLS], d, final, mask[:, 0:COLS], ALU.not_equal, ALU.mult))
            step(V.scalar_tensor_tensor(nxtf[:, 0:COLS], d, -float(SKIP), mask[:, 0:COLS], ALU.add, ALU.mult))
            V.tensor_scalar(put[:, 0:COLS], nxtf[:, 0:COLS], sorted_[:, :], float(SKIP), ALU.mult, ALU.add)
            step(V.tensor_tensor(mask[:, 1:COLS], dstf[:, 1:COLS], dstf[:, 0:COLS - 1], ALU.is_equal))
            V.tensor_scalar(goes_on[:, 1:COLS], mask[:, 1:COLS], sorted_[:, :], None, ALU.mult)
            V.tensor_scalar(in_head[:, 0:COLS], d, first, None, ALU.is_equal)
            V.tensor_copy(left[:, :], dstf[:, :]).then_inc(pre, 1)
            dve.wait_ge(pre, 1)

            for j in range(3):
                moments(0, j, 0)
                moments(0, j, 1)
                if j == 0:
                    V.tensor_copy(rx[:, :], xd[:, 0, :]).then_inc(kept, 1)
                spreads(0, j)
                if j < 2:
                    for stage in (newton0, newton1, newton2, shifts):
                        stage(0, j)
            lap(0)
            lap(1)
            with dve.Fori(2, LAPS - 1) as o:
                lap(o)
            lap(LAPS - 1)
            work(LAPS, 0)

            recs = [0]

            def rec(ins):
                recs[0] += 1
                ins.then_inc(rec_step, 1)
                dve.wait_ge(rec_step, recs[0])

            dve.wait_ge(head_ok, TILES // 2)
            V.tensor_tensor(rmat[:, 0, :], head[:, 0, :], head[:, 1, :], ALU.add)
            V.tensor_copy(rmat[:, 1, :], run[:, COLS * C:TILES * C])
            V.tensor_copy(rmat[:, 2, :], run[:, TILES * C:(TILES + 1) * C])
            for g in range(3):
                last = V.tensor_scalar(diag[:, g, :], ident[:, :], ids[:, g:g + 1], None, ALU.mult)
            last.then_inc(rec_ids, 1)
            dve.wait_ge(rec_b, 1)
            for h in range(3):
                last = V.tensor_scalar(eq[:, h, :], ps_t[:, 0, 0, 0:3 * P], ids[:, h:h + 1], None, ALU.is_equal)
            rec(last)
            for g in range(3):
                last = V.tensor_tensor(eqb[:, g, :], eq[:, g, g * P:(g + 1) * P], before[:, :], ALU.mult)
            last.then_inc(rec_eq, 1)
            dve.wait_ge(rec_sum, 1)
            sums3 = ps_p[:, 0, 0, 0:3 * C].rearrange("p (k c) -> p k c", k=3)
            rec(V.tensor_scalar(rz[:, 0, :, :], sums3[:, :, D:C], 1e-6, None, ALU.add))
            rec(V.reciprocal(rz[:, 1, :, :], rz[:, 0, :, :]))
            rec(V.tensor_tensor(by_head(rh[:, :, :]), by_head(sums3[:, :, 0:D]), wide(rz[:, 1, :, :]), ALU.mult))
            dve.wait_ge(kept, 1)
            V.tensor_tensor(rrow[:, 0, :], rh[:, 0, :], rx[:, :], ALU.add)
            V.tensor_tensor(rrow[:, 1:3, :], rh[:, 1:3, :], xd[:, LAP - 2:LAP, :], ALU.add)
            V.tensor_scalar(rsel[:, 0, :], ps_p[:, 0, 1, 0:3], 0.0, None, ALU.is_equal)
            V.tensor_scalar(rsel[:, 1, :], ids[:, :], 0.0, sorted_[:, :], ALU.is_ge, ALU.mult)
            rec(V.tensor_scalar(rsel[:, 2, :], ids[:, :], -float(SKIP), None, ALU.add))
            rec(V.tensor_tensor(rsel[:, 0, :], rsel[:, 0, :], rsel[:, 1, :], ALU.mult))
            rec(V.tensor_tensor(rsel[:, 3, :], rsel[:, 0, :], rsel[:, 2, :], ALU.mult))
            V.tensor_scalar(rput[:, :], rsel[:, 3, :], float(SKIP), None, ALU.add).then_inc(rec_ok, 1)

            dve.sem_inc(flag, 1)
            unsorted = dve.value_load(bad[0:1, 0:1])
            with dve.If(unsorted != 0):
                V.memset(fz[:, :, :], 0.0).then_inc(facc_free, 1)
                GROUPS = TILES // FG
                with dve.Fori(0, FTILES) as n:
                    with dve.Fori(0, GROUPS // 2) as g:
                        for b in range(2):
                            dve.wait_ge(hot_free, n * GROUPS + g * 2 + b + 1)
                            V.tensor_tensor(
                                hot[b][:, :, :],
                                node[:, :].unsqueeze(1).to_broadcast([P, FG, FN]),
                                left[:, bass.ds(g * (2 * FG) + b * FG, FG)].unsqueeze(2).to_broadcast([P, FG, FN]),
                                ALU.is_equal).then_inc(hot_ok, 1)
                    dve.wait_ge(facc_ok, n + 1)
                    V.tensor_scalar(left[:, :], left[:, :], -float(FN), None, ALU.add)
                    acc = ps_t[0:FN, 1, 0, 0:C]
                    V.tensor_scalar(fz[:, 0, :], acc[:, D:C], 1e-6, None, ALU.add).then_inc(f_step, 1)
                    dve.wait_ge(f_step, n * 2 + 1)
                    V.reciprocal(fz[:, 1, :], fz[:, 0, :]).then_inc(f_step, 1)
                    dve.wait_ge(f_step, n * 2 + 2)
                    V.tensor_tensor(fh[:, :].rearrange("p (h d) -> p h d", d=HD),
                                    acc[:, 0:D].rearrange("p (h d) -> p h d", d=HD),
                                    fz[:, 1, :].unsqueeze(2).to_broadcast([FN, H, HD]),
                                    ALU.mult).then_inc(facc_free, 1)
                    dve.wait_ge(facc_free, n + 2)
                    dve.wait_ge(fx_in, (n + 1) * 16)
                    V.tensor_tensor(fo[:, :], fh[:, :], fx[:, :], ALU.add).then_inc(fo_ok, 1)


_INS = ["x", "src", "dst", "edge_attr_96", "L0_gnn_Wq", "L0_gnn_bq", "L0_gnn_Wk", "L0_gnn_bk",
        "L0_gnn_We", "L0_gnn_be", "L0_gnn_Wv", "L0_gnn_bv"]


def kernel(**inputs):
    import numpy as _np
    import concourse.bacc as _bacc
    from concourse import mybir as _mybir
    from concourse.bass_utils import run_bass_kernel_spmd as _run

    nc = _bacc.Bacc("TRN2", target_bir_lowering=False, num_devices=1)
    arrays, args = {}, []
    for name in _INS:
        a = _np.ascontiguousarray(inputs[name])
        arrays[f"in_{name}_dram"] = a
        args.append(nc.dram_tensor(f"in_{name}_dram", a.shape, _mybir.dt.from_np(a.dtype), kind="ExternalInput").ap())
    shape = inputs["x"].shape
    out = nc.dram_tensor("out_dram", shape, _mybir.dt.float32, kind="ExternalOutput").ap()
    gnn_edge_attention(nc, *args, out)
    r = _run(nc, [arrays], core_ids=[0])
    return r.results[0]["out_dram"]
```
